# Optimizing a Trainium2 kernel written in Bass

```python
import numpy as np
import jax
import jax.numpy as jnp

def _softmax(x, axis=-1):
    return jax.nn.softmax(x, axis=axis)

def _gelu(x):
    return jax.nn.gelu(x, approximate=True)

def _silu(x):
    return jax.nn.silu(x)

def _sigmoid(x):
    return jax.nn.sigmoid(x)

def _layernorm(x, axis=-1, eps=1e-05):
    m = jnp.mean(x, axis=axis, keepdims=True)
    v = jnp.var(x, axis=axis, keepdims=True)
    return (x - m) / jnp.sqrt(v + eps)

def _scatter_add(tgt, idx, src, axis=0):
    return tgt.at[idx].add(src)

def _segment_sum(src, seg, n):
    return jax.ops.segment_sum(src, seg, n)
kernel_name = 'mk_dlrm_tower_d1_rec_r8_09a21f'

def setup_inputs(seed: int=0):
    np.random.seed(seed)
    _w = jnp.asarray

    def _rec_inputs():
        import jax
        import jax.numpy as jnp
        _tk = jax.random.key(seed)
        dense_ctx = jax.random.normal(jax.random.fold_in(_tk, 190), (1024, 16), jnp.float32)
        ids = jnp.stack([jax.random.randint(jax.random.fold_in(_tk, 200 + f), (1024,), 0, v, jnp.int32) for f, v in enumerate([1000, 1000, 12500, 1250, 125000, 125000, 1000, 1250, 125000, 1000, 12500, 12500, 1000, 1250, 1250, 1250, 12500, 12500, 1250, 1000, 1250, 12500, 12500, 1000, 1250, 1250, 12500, 1000, 1000, 1000, 1000, 1000])], axis=1)
        tbl_0 = 0.05 * jax.random.normal(jax.random.fold_in(_tk, 500 + 0), (1000, 64), jnp.float32)
        tbl_1 = 0.05 * jax.random.normal(jax.random.fold_in(_tk, 500 + 1), (1000, 64), jnp.float32)
        tbl_2 = 0.05 * jax.random.normal(jax.random.fold_in(_tk, 500 + 2), (12500, 64), jnp.float32)
        tbl_3 = 0.05 * jax.random.normal(jax.random.fold_in(_tk, 500 + 3), (1250, 64), jnp.float32)
        tbl_4 = 0.05 * jax.random.normal(jax.random.fold_in(_tk, 500 + 4), (125000, 64), jnp.float32)
        tbl_5 = 0.05 * jax.random.normal(jax.random.fold_in(_tk, 500 + 5), (125000, 64), jnp.float32)
        tbl_6 = 0.05 * jax.random.normal(jax.random.fold_in(_tk, 500 + 6), (1000, 64), jnp.float32)
        tbl_7 = 0.05 * jax.random.normal(jax.random.fold_in(_tk, 500 + 7), (1250, 64), jnp.float32)
        tbl_8 = 0.05 * jax.random.normal(jax.random.fold_in(_tk, 500 + 8), (125000, 64), jnp.float32)
        tbl_9 = 0.05 * jax.random.normal(jax.random.fold_in(_tk, 500 + 9), (1000, 64), jnp.float32)
        tbl_10 = 0.05 * jax.random.normal(jax.random.fold_in(_tk, 500 + 10), (12500, 64), jnp.float32)
        tbl_11 = 0.05 * jax.random.normal(jax.random.fold_in(_tk, 500 + 11), (12500, 64), jnp.float32)
        tbl_12 = 0.05 * jax.random.normal(jax.random.fold_in(_tk, 500 + 12), (1000, 64), jnp.float32)
        tbl_13 = 0.05 * jax.random.normal(jax.random.fold_in(_tk, 500 + 13), (1250, 64), jnp.float32)
        tbl_14 = 0.05 * jax.random.normal(jax.random.fold_in(_tk, 500 + 14), (1250, 64), jnp.float32)
        tbl_15 = 0.05 * jax.random.normal(jax.random.fold_in(_tk, 500 + 15), (1250, 64), jnp.float32)
        tbl_16 = 0.05 * jax.random.normal(jax.random.fold_in(_tk, 500 + 16), (12500, 64), jnp.float32)
        tbl_17 = 0.05 * jax.random.normal(jax.random.fold_in(_tk, 500 + 17), (12500, 64), jnp.float32)
        tbl_18 = 0.05 * jax.random.normal(jax.random.fold_in(_tk, 500 + 18), (1250, 64), jnp.float32)
        tbl_19 = 0.05 * jax.random.normal(jax.random.fold_in(_tk, 500 + 19), (1000, 64), jnp.float32)
        tbl_20 = 0.05 * jax.random.normal(jax.random.fold_in(_tk, 500 + 20), (1250, 64), jnp.float32)
        tbl_21 = 0.05 * jax.random.normal(jax.random.fold_in(_tk, 500 + 21), (12500, 64), jnp.float32)
        tbl_22 = 0.05 * jax.random.normal(jax.random.fold_in(_tk, 500 + 22), (12500, 64), jnp.float32)
        tbl_23 = 0.05 * jax.random.normal(jax.random.fold_in(_tk, 500 + 23), (1000, 64), jnp.float32)
        tbl_24 = 0.05 * jax.random.normal(jax.random.fold_in(_tk, 500 + 24), (1250, 64), jnp.float32)
        tbl_25 = 0.05 * jax.random.normal(jax.random.fold_in(_tk, 500 + 25), (1250, 64), jnp.float32)
        tbl_26 = 0.05 * jax.random.normal(jax.random.fold_in(_tk, 500 + 26), (12500, 64), jnp.float32)
        tbl_27 = 0.05 * jax.random.normal(jax.random.fold_in(_tk, 500 + 27), (1000, 64), jnp.float32)
        tbl_28 = 0.05 * jax.random.normal(jax.random.fold_in(_tk, 500 + 28), (1000, 64), jnp.float32)
        tbl_29 = 0.05 * jax.random.normal(jax.random.fold_in(_tk, 500 + 29), (1000, 64), jnp.float32)
        tbl_30 = 0.05 * jax.random.normal(jax.random.fold_in(_tk, 500 + 30), (1000, 64), jnp.float32)
        tbl_31 = 0.05 * jax.random.normal(jax.random.fold_in(_tk, 500 + 31), (1000, 64), jnp.float32)
        _rk = jax.random.fold_in(_tk, 7)
        W_top1 = 0.0441942 * jax.random.normal(jax.random.fold_in(_tk, 801), (512, 512), jnp.float32)
        W_top2 = 0.0441942 * jax.random.normal(jax.random.fold_in(_tk, 802), (512, 256), jnp.float32)
        W_top3 = 0.0625 * jax.random.normal(jax.random.fold_in(_tk, 803), (256, 1), jnp.float32)
        b_top1 = jnp.zeros((512,), jnp.float32)
        b_top2 = jnp.zeros((256,), jnp.float32)
        return (dense_ctx, ids, tbl_0, tbl_1, tbl_2, tbl_3, tbl_4, tbl_5, tbl_6, tbl_7, tbl_8, tbl_9, tbl_10, tbl_11, tbl_12, tbl_13, tbl_14, tbl_15, tbl_16, tbl_17, tbl_18, tbl_19, tbl_20, tbl_21, tbl_22, tbl_23, tbl_24, tbl_25, tbl_26, tbl_27, tbl_28, tbl_29, tbl_30, tbl_31, W_top1, b_top1, W_top2, b_top2, W_top3)
    dense_ctx, ids, tbl_0, tbl_1, tbl_2, tbl_3, tbl_4, tbl_5, tbl_6, tbl_7, tbl_8, tbl_9, tbl_10, tbl_11, tbl_12, tbl_13, tbl_14, tbl_15, tbl_16, tbl_17, tbl_18, tbl_19, tbl_20, tbl_21, tbl_22, tbl_23, tbl_24, tbl_25, tbl_26, tbl_27, tbl_28, tbl_29, tbl_30, tbl_31, W_top1, b_top1, W_top2, b_top2, W_top3 = _rec_inputs()

    def _L0_rec_setup():
        import jax, jax.numpy as jnp
        import numpy as np
        key = jax.random.key(seed)
        k1, k2 = jax.random.split(key)
        B, F, D = (512, 32, 64)
        P = F * (F - 1) // 2
        x = jax.random.normal(k1, (B, F, D), dtype=jnp.float32)
        W = jax.random.normal(k2, (P, D, D), dtype=jnp.float32) * (1.0 / np.sqrt(D))
        return {'x': x, 'W': W}
    _L0_rec_all = _L0_rec_setup()
    _L0_rec_in = {k: v for k, v in _L0_rec_all.items() if k in ('W',)}
    del _L0_rec_all
    return {'dense_ctx': dense_ctx, 'ids': ids, 'tbl_0': tbl_0, 'tbl_1': tbl_1, 'tbl_2': tbl_2, 'tbl_3': tbl_3, 'tbl_4': tbl_4, 'tbl_5': tbl_5, 'tbl_6': tbl_6, 'tbl_7': tbl_7, 'tbl_8': tbl_8, 'tbl_9': tbl_9, 'tbl_10': tbl_10, 'tbl_11': tbl_11, 'tbl_12': tbl_12, 'tbl_13': tbl_13, 'tbl_14': tbl_14, 'tbl_15': tbl_15, 'tbl_16': tbl_16, 'tbl_17': tbl_17, 'tbl_18': tbl_18, 'tbl_19': tbl_19, 'tbl_20': tbl_20, 'tbl_21': tbl_21, 'tbl_22': tbl_22, 'tbl_23': tbl_23, 'tbl_24': tbl_24, 'tbl_25': tbl_25, 'tbl_26': tbl_26, 'tbl_27': tbl_27, 'tbl_28': tbl_28, 'tbl_29': tbl_29, 'tbl_30': tbl_30, 'tbl_31': tbl_31, 'W_top1': W_top1, 'b_top1': b_top1, 'W_top2': W_top2, 'b_top2': b_top2, 'W_top3': W_top3, 'L0_rec_W': _L0_rec_in['W']}

def reference(dense_ctx, ids, tbl_0, tbl_1, tbl_2, tbl_3, tbl_4, tbl_5, tbl_6, tbl_7, tbl_8, tbl_9, tbl_10, tbl_11, tbl_12, tbl_13, tbl_14, tbl_15, tbl_16, tbl_17, tbl_18, tbl_19, tbl_20, tbl_21, tbl_22, tbl_23, tbl_24, tbl_25, tbl_26, tbl_27, tbl_28, tbl_29, tbl_30, tbl_31, W_top1, b_top1, W_top2, b_top2, W_top3, L0_rec_W):
    import jax
    import jax.numpy as jnp

    def _L0_rec_ref(x, W):
        import jax, jax.numpy as jnp
        import numpy as np
        F = x.shape[1]
        idx_i, idx_j = np.triu_indices(F, k=1)
        xi = x[:, idx_i, :]
        xj = x[:, idx_j, :]
        left = jnp.einsum('bpd,pde->bpe', xi, W)
        out = jnp.sum(left * xj, axis=-1)
        return out
    e = jnp.stack([tbl_0[ids[:, 0]], tbl_1[ids[:, 1]], tbl_2[ids[:, 2]], tbl_3[ids[:, 3]], tbl_4[ids[:, 4]], tbl_5[ids[:, 5]], tbl_6[ids[:, 6]], tbl_7[ids[:, 7]], tbl_8[ids[:, 8]], tbl_9[ids[:, 9]], tbl_10[ids[:, 10]], tbl_11[ids[:, 11]], tbl_12[ids[:, 12]], tbl_13[ids[:, 13]], tbl_14[ids[:, 14]], tbl_15[ids[:, 15]], tbl_16[ids[:, 16]], tbl_17[ids[:, 17]], tbl_18[ids[:, 18]], tbl_19[ids[:, 19]], tbl_20[ids[:, 20]], tbl_21[ids[:, 21]], tbl_22[ids[:, 22]], tbl_23[ids[:, 23]], tbl_24[ids[:, 24]], tbl_25[ids[:, 25]], tbl_26[ids[:, 26]], tbl_27[ids[:, 27]], tbl_28[ids[:, 28]], tbl_29[ids[:, 29]], tbl_30[ids[:, 30]], tbl_31[ids[:, 31]]], axis=1)
    z = _L0_rec_ref(e, L0_rec_W)
    z = z.reshape(z.shape[0], -1)
    h = jnp.concatenate([z, dense_ctx], axis=1)
    h = jnp.maximum(h @ W_top1 + b_top1, 0.0)
    h = jnp.maximum(h @ W_top2 + b_top2, 0.0)
    y = h @ W_top3
    return y

_drawn_inputs = setup_inputs


def setup_inputs(seed=0):
    import zlib

    import numpy as np

    out = dict(_drawn_inputs(seed))
    spreads = {'b_top1': (0.0, 0.1), 'b_top2': (0.0, 0.1)}
    factors = {}
    for name, (base, spread) in spreads.items():
        noise = np.random.default_rng([zlib.crc32(name.encode()), seed]).standard_normal(out[name].shape)
        drawn = base * np.exp(spread * noise) if base else spread * noise
        out[name] = jnp.asarray(drawn.astype(out[name].dtype))
    for name, factor in factors.items():
        out[name] = (out[name] * factor).astype(out[name].dtype)
    return out
```

```python
from contextlib import ExitStack

import numpy as np

import concourse.bass as bass
from concourse import mybir

ALU = mybir.AluOpType
ACT = mybir.ActivationFunctionType
F32 = mybir.dt.float32
F32R = mybir.dt.float32r

P = 128
B = 1024
F = 32
D = 64
FP = F // 2
HB = 512
HALVES = B // HB
BT = HB // P
NPAIR = F * (F - 1) // 2
NCTX = 16
STEPS = FP * HALVES

UNITS = 2 * NPAIR // 4 + FP // 2
CHUNK = 64
CHUNKS = UNITS // CHUNK
H1, H2 = 512, 256

RING = 3
PRODS = 6
REDUCE_LAG = 2
REDUCE_BATCH = 4
RAW = 2
WSLOTS = 4
GATHERS = 4


def first_pair(i):
    return sum(F - 1 - a for a in range(i))


def step_of(g):
    return g // FP, FP - 1 - g % FP


def weights_of_step(g):
    h, m = step_of(g)
    return [(i, (F - 1) * h + F - 2 - i) for i in (2 * m + 1, 2 * m) if i < F - 1]


def groups_of_step(m):
    return [m] + list(range(FP - 1, m, -1))


def row_fields():
    rows = []
    for g in range(FP):
        m = step_of(g)[1]
        for k in groups_of_step(m):
            if k == m:
                rows.append((NPAIR + m, first_pair(2 * m)))
            else:
                for i in (2 * m, 2 * m + 1):
                    a = first_pair(i) + 2 * k - i - 1
                    rows.append((a, a + 1))
    return rows


def z_row(u):
    return 32 * (u % 4) + 2 * (u % CHUNK // 4)


def w1_rows():
    index = np.zeros((P, CHUNKS), np.int32)
    for u, (a, b) in enumerate(row_fields()):
        index[z_row(u), u // CHUNK] = a
        index[z_row(u) + 1, u // CHUNK] = b
    return index


def make_plan():
    plan, groups, units = [], [], 0
    done, diagonal = 0, -1

    def reduce_up_to(n):
        nonlocal done
        while done < n:
            plan.append(("reduce", done))
            done += 1

    plan += [("context", h) for h in range(HALVES)]
    plan += [("transpose", 0), ("split_x", 0)] + [("split_w", x) for x in weights_of_step(0)]
    for g in range(STEPS):
        h, m = step_of(g)
        ks = groups_of_step(m)
        nxt = []
        if g + 1 < STEPS:
            nxt = [("split_w", x) for x in weights_of_step(g + 1)]
            nxt = [("transpose", g + 1)] + nxt[:-1] + [("split_x", g + 1)] + nxt[-1:]
        at = max(0, len(ks) // 2 - 2) if len(ks) >= 6 else len(ks) - 1
        for n, k in enumerate(ks):
            own = 1 if k == m else 2
            if k == m:
                reduce_up_to(diagonal + 1)
                diagonal = len(groups)
            groups.append((g, k, units))
            units += own
            plan.append(("project", len(groups) - 1))
            if len(groups) - done >= REDUCE_LAG + REDUCE_BATCH:
                reduce_up_to(done + REDUCE_BATCH)
            if nxt and n >= at:
                plan.append(nxt.pop(0))
        plan += nxt
        if h == 1 and g % FP in (1, 2, 3):
            reduce_up_to(sum(FP - step_of(a)[1] for a in range(FP)))
            plan.append((f"layer{g % FP}", 0))
    reduce_up_to(len(groups))
    plan += [(f"layer{n}", HALVES - 1) for n in (1, 2, 3)]
    return plan, groups


def dlrm_tower(nc, dense_ctx, ids, tables, W, W1, b1, W2, b2, W3, w1_index, out):
    plan, groups = make_plan()
    last_of_chunk = {}
    for G, (g, k, u) in enumerate(groups):
        n = 1 if k == step_of(g)[1] else 2
        for x in range(u, u + n):
            if x % CHUNK == CHUNK - 1:
                last_of_chunk[G] = x // CHUNK
    ctx = ExitStack()
    with ctx:
        def sb(name, shape, dt=F32):
            return ctx.enter_context(nc.sbuf_tensor(name, shape, dt))

        def sem(name):
            return ctx.enter_context(nc.semaphore(name))

        ids_sb = sb("ids_sb", [P, HALVES * BT, F], mybir.dt.int32)
        w1_index_sb = sb("w1_index_sb", [P, CHUNKS], mybir.dt.int32)
        context_rows = sb("context_rows", [P, HALVES * BT, NCTX])
        gathered = sb("gathered", [P, GATHERS, BT, 2, D])
        raw_w = sb("raw_w", [D, RAW, F - 1, D])
        w_split = sb("w_split", [P, WSLOTS, F, D], F32R)
        x_hi = sb("x_hi", [P, 2, 2, HB], F32R)
        x_lo = sb("x_lo", [P, 2, 2, HB], F32R)
        X = sb("X", [P, FP, HB])
        products = sb("products", [P, PRODS, 2, HB])
        diagonal = sb("diagonal", [P, HALVES, HB])
        ident = sb("ident", [P, P])
        ones_window = sb("ones_window", [P, 62])
        diag_window = sb("diag_window", [P, FP, 62])
        z = sb("z", [P, CHUNKS, HB])
        h1 = sb("h1", [P, H1 // P, HB])
        h2 = sb("h2", [P, H2 // P, HB])
        w1_sb = sb("w1_sb", [P, CHUNKS, H1])
        w2_sb = sb("w2_sb", [P, H1 // P, H2])
        w3_sb = sb("w3_sb", [P, H2 // P])
        b1_sb = sb("b1_sb", [P, H1 // P])
        b2_sb = sb("b2_sb", [P, H2 // P])
        y = sb("y", [1, HALVES, HB])

        left = ctx.enter_context(nc.psum_tensor("left", [P, RING, 2, HB], F32))
        xT = ctx.enter_context(nc.psum_tensor("xT", [P, HB], F32))
        z_sum = ctx.enter_context(nc.psum_tensor("z_sum", [P, HB], F32))

        ids_loaded = sem("ids_loaded")
        index_loaded = sem("index_loaded")
        context_loaded = sem("context_loaded")
        w1_loaded = sem("w1_loaded")
        mlp_loaded = sem("mlp_loaded")
        raw_loaded = [sem(f"raw_loaded{r}") for r in range(RAW)]
        rows_gathered = [sem(f"rows_gathered{r}") for r in range(GATHERS)]
        constants_zeroed = sem("constants_zeroed")
        ident_ready = sem("ident_ready")
        windows_ready = sem("windows_ready")
        diagonal_zeroed = sem("diagonal_zeroed")
        split_zeroed = sem("split_zeroed")
        transposed = sem("transposed")
        context_placed = sem("context_placed")
        x_hi_natural = sem("x_hi_natural")
        x_copied = sem("x_copied")
        x_lo_natural = sem("x_lo_natural")
        x_split = sem("x_split")
        w_hi_ready = sem("w_hi_ready")
        w_lo_ready = sem("w_lo_ready")
        projected = sem("projected")
        multiplied = sem("multiplied")
        reduced = sem("reduced")
        z_copied = sem("z_copied")
        layer_summed = sem("layer_summed")
        layer_copied = sem("layer_copied")
        y_stored = sem("y_stored")

        slot, freed, use, mlp_piece = {}, [], 0, 0
        for what, n in plan:
            if what == "project":
                slot[what, n] = use
                freed.append((multiplied, n + 1))
                use += 1
            elif what.startswith("layer"):
                for piece in range(2 if what == "layer1" else 1):
                    slot[what, n, piece] = use
                    mlp_piece += 1
                    freed.append((layer_copied, mlp_piece))
                    use += 1

        def claim(eng, n):
            if n >= RING:
                eng.wait_ge(*freed[n - RING])
            return n % RING

        def groups_through(g):
            return sum(1 for x in groups if x[0] <= g)

        diag_group = [next(G for G, x in enumerate(groups) if x[0] == g) for g in range(STEPS)]

        last_use = {}
        for G, (g, k, u) in enumerate(groups):
            last_use[step_of(g)[0], k] = G

        def units_through(G):
            g, k, u = groups[G]
            return u + (1 if k == step_of(g)[1] else 2)

        block = ctx.enter_context(nc.Block())

        @block.sync
        def _(sp):
            sp.dma_start(ids_sb[:, :, :], ids.rearrange("(t p) f -> p t f", p=P)).then_inc(ids_loaded, 16)
            sp.dma_start(context_rows[:, :, :], dense_ctx.rearrange("(t p) f -> p t f", p=P)).then_inc(context_loaded, 16)
            sp.dma_start(w1_index_sb[:, :], w1_index).then_inc(index_loaded, 16)
            for g in range(STEPS):
                for i, n in weights_of_step(g):
                    pairs = F - 1 - i
                    if n >= RAW:
                        sp.wait_ge(w_hi_ready, n - RAW + 1)
                        sp.wait_ge(w_lo_ready, n - RAW + 1)
                    a = first_pair(i)
                    sp.dma_start(raw_w[:, n % RAW, 0:pairs, :],
                                 W[a:a + pairs].rearrange("p d e -> d p e")).then_inc(raw_loaded[n % RAW], 16)
                if g == 3:
                    sp.dma_start(w2_sb[:, :, :], W2.rearrange("(c p) n -> p c n", p=P)).then_inc(mlp_loaded, 16)
                    with nc.allow_non_contiguous_dma(reason="a few hundred words"):
                        sp.dma_start(w3_sb[:, :], W3.rearrange("(c p) n -> p (c n)", p=P)).then_inc(mlp_loaded, 16)
                        sp.dma_start(b1_sb[:, :], b1.rearrange("(c p) -> p c", p=P)).then_inc(mlp_loaded, 16)
                        sp.dma_start(b2_sb[:, :], b2.rearrange("(c p) -> p c", p=P)).then_inc(mlp_loaded, 16)
            for h in range(HALVES):
                sp.wait_ge(layer_copied, 4 * (h + 1))
                sp.dma_start(out[h * HB:(h + 1) * HB, :].rearrange("b o -> o b"), y[:, h, :]).then_inc(y_stored, 16)
            sp.wait_ge(y_stored, 16 * HALVES)

        @block.gpsimd
        def _(pool):
            nc.gpsimd.memset(ident[:, :], 0.0).then_inc(constants_zeroed, 1)
            nc.gpsimd.memset(ones_window[:, :], 0.0).then_inc(constants_zeroed, 1)
            nc.gpsimd.memset(diag_window[:, :, :], 0.0).then_inc(constants_zeroed, 1)
            pool.wait_ge(constants_zeroed, 3)
            nc.gpsimd.affine_select(out=ident[:, :], in_=ident[:, :], compare_op=ALU.not_equal, fill=1.0, base=0,
                                    pattern=[[-1, P]], channel_multiplier=1).then_inc(ident_ready, 1)
            pool.wait_ge(ids_loaded, 16)
            for g in range(STEPS):
                h, m = step_of(g)
                if g >= GATHERS:
                    pool.wait_ge(transposed, HALVES + g - GATHERS + 1)
                for odd in (0, 1):
                    for t in range(BT):
                        f = 2 * m + odd
                        pool.indirect_dma_start(
                            out=gathered[:, g % GATHERS, t, odd, :], out_offset=None, in_=tables[f],
                            in_offset=bass.IndirectOffsetOnAxis(ap=ids_sb[:, h * BT + t, f:f + 1], axis=0),
                        ).then_inc(rows_gathered[g % GATHERS], 16)
                if g == 6:
                    pool.wait_ge(index_loaded, 16)
                    for c in range(CHUNKS):
                        pool.indirect_dma_start(
                            out=w1_sb[:, c, :], out_offset=None, in_=W1,
                            in_offset=bass.IndirectOffsetOnAxis(ap=w1_index_sb[:, c:c + 1], axis=0),
                        ).then_inc(w1_loaded, 16)

        @block.vector
        def _(dve):
            nc.vector.memset(diagonal[:, :, :], 0.0).then_inc(diagonal_zeroed, 1)
            nc.vector.memset(w_split[:, 0:WSLOTS:2, 0, :].bitcast(F32), 0.0).then_inc(split_zeroed, 1)
            dve.wait_ge(constants_zeroed, 3)
            nc.vector.memset(ones_window[0:D, 30:31], 1.0).then_inc(windows_ready, 1)
            nc.vector.memset(ones_window[D:P, 31:32], 1.0).then_inc(windows_ready, 1)
            nc.vector.memset(diag_window[D:P, :, 31:32], 1.0).then_inc(windows_ready, 1)
            dve.wait_ge(ident_ready, 1)
            nc.vector.tensor_copy(diag_window[0:NCTX, :, 30], ident[0:NCTX, 0:FP]).then_inc(windows_ready, 1)

            def split_x(g):
                dve.wait_ge(x_hi_natural, 2 * (g + 1))
                dve.wait_ge(x_copied, g + 1)
                m = step_of(g)[1]
                for odd in (0, 1):
                    at = slice(D * odd, D * odd + D)
                    nc.vector.tensor_tensor(x_lo[at, g % 2, odd, :], X[at, m, :], x_hi[at, g % 2, odd, :].bitcast(F32),
                                            ALU.subtract).then_inc(x_lo_natural, 1)

            def split_w(i, n):
                dve.wait_ge(w_hi_ready, n + 1)
                a, pairs = 1 - i % 2, F - 1 - i
                nc.vector.tensor_tensor(w_split[D:P, i % WSLOTS, a:a + pairs, :], raw_w[:, n % RAW, 0:pairs, :],
                                        w_split[0:D, i % WSLOTS, a:a + pairs, :].bitcast(F32),
                                        ALU.subtract).then_inc(w_lo_ready, 1)

            def multiply(G):
                g, k, u = groups[G]
                h, m = step_of(g)
                s = slot["project", G] % RING
                dve.wait_ge(projected, G + 1)
                if k == m:
                    if g % FP == 0:
                        dve.wait_ge(context_placed, h + 1)
                    else:
                        dve.wait_ge(reduced, units_through(diag_group[g - 1]))
                    nc.vector.tensor_tensor(diagonal[D:P, h, :], left[D:P, s, 0, :], X[D:P, k, :],
                                            ALU.mult).then_inc(multiplied, 1)
                    return
                if G >= PRODS:
                    dve.wait_ge(reduced, units_through(G - PRODS))
                nc.vector.tensor_tensor(products[:, G % PRODS, :, :], left[:, s, :, :],
                                        X[:, k:k + 1, :].to_broadcast([P, 2, HB]), ALU.mult).then_inc(multiplied, 1)

            for what, n in plan:
                if what == "split_x":
                    split_x(n)
                elif what == "split_w":
                    split_w(*n)
                elif what == "project":
                    multiply(n)

        @block.scalar
        def _(act):
            def place_context(h):
                act.wait_ge(transposed, h + 1)
                act.wait_ge(diagonal_zeroed, 1)
                nc.scalar.activation(diagonal[0:NCTX, h, :], xT[0:NCTX, :], ACT.Copy).then_inc(context_placed, 1)

            def read_transposed(g):
                h, m = step_of(g)
                act.wait_ge(transposed, HALVES + g + 1)
                if g >= 2:
                    act.wait_ge(projected, groups_through(g - 2))
                for odd in (0, 1):
                    at = slice(D * odd, D * odd + D)
                    nc.scalar.activation(x_hi[at, g % 2, odd, :], xT[at, :], ACT.Copy).then_inc(x_hi_natural, 1)
                if h:
                    act.wait_ge(multiplied, last_use[h - 1, m] + 1)
                nc.scalar.activation(X[:, m, :], xT[:, :], ACT.Copy).then_inc(x_copied, 1)
                for odd in (0, 1):
                    at, other = slice(D * odd, D * odd + D), slice(D - D * odd, P - D * odd)
                    nc.scalar.activation(x_hi[other, g % 2, odd, :], xT[at, :], ACT.Copy).then_inc(x_split, 1)

            def double_lo(g):
                act.wait_ge(x_lo_natural, 2 * (g + 1))
                for odd in (0, 1):
                    at, other = slice(D * odd, D * odd + D), slice(D - D * odd, P - D * odd)
                    nc.scalar.activation(x_lo[other, g % 2, odd, :], x_lo[at, g % 2, odd, :].bitcast(F32),
                                         ACT.Copy).then_inc(x_split, 1)

            def round_w(i, n):
                g = FP * (n // (F - 1)) + FP - 1 - i // 2
                act.wait_ge(raw_loaded[n % RAW], 16 * (n // RAW + 1))
                if g >= 2:
                    act.wait_ge(projected, groups_through(g - 2))
                a, pairs = 1 - i % 2, F - 1 - i
                nc.scalar.activation(w_split[0:D, i % WSLOTS, a:a + pairs, :], raw_w[:, n % RAW, 0:pairs, :],
                                     ACT.Copy).then_inc(w_hi_ready, 1)

            def copy_z(G):
                c = last_of_chunk[G]
                act.wait_ge(reduced, CHUNK * (c + 1))
                if c >= CHUNKS:
                    act.wait_ge(layer_summed, 4 * (c // CHUNKS - 1) + 2)
                nc.scalar.activation(z[:, c % CHUNKS, :], z_sum[:, :], ACT.Copy).then_inc(z_copied, 1)

            def relu(what, h, piece):
                s = slot[what, h, piece] % RING
                n = 4 * h + {"layer1": 0, "layer2": 2}[what] + piece
                act.wait_ge(layer_summed, n + 1)
                act.wait_ge(mlp_loaded, 64)
                for j in (0, 1):
                    c = 2 * piece + j
                    to, bias = (h1, b1_sb) if what == "layer1" else (h2, b2_sb)
                    ins = nc.scalar.activation(to[:, c, :], left[:, s, j, :], ACT.Relu, bias=bias[:, c:c + 1])
                ins.then_inc(layer_copied, 1)

            for what, n in plan:
                if what == "context":
                    place_context(n)
                elif what == "transpose":
                    read_transposed(n)
                elif what == "split_x":
                    double_lo(n)
                elif what == "split_w":
                    round_w(*n)
                elif what == "reduce" and n in last_of_chunk:
                    copy_z(n)
                elif what in ("layer1", "layer2"):
                    for piece in range(2 if what == "layer1" else 1):
                        relu(what, n, piece)
                elif what == "layer3":
                    act.wait_ge(layer_summed, 4 * n + 4)
                    nc.scalar.activation(y[:, n, :], left[0:1, slot[what, n, 0] % RING, 0, :],
                                         ACT.Copy).then_inc(layer_copied, 1)

        @block.tensor
        def _(pe):
            def transpose_context(h):
                if h == 0:
                    pe.wait_ge(ident_ready, 1)
                    pe.wait_ge(context_loaded, 16)
                else:
                    pe.wait_ge(context_placed, h)
                for t in range(BT):
                    ins = nc.tensor.transpose(xT[0:NCTX, t * P:(t + 1) * P], context_rows[:, h * BT + t, :], ident[:, :])
                ins.then_inc(transposed, 1)

            def transpose_x(g):
                pe.wait_ge(rows_gathered[g % GATHERS], 16 * 2 * BT * (g // GATHERS + 1))
                if g == 0:
                    pe.wait_ge(context_placed, HALVES)
                else:
                    pe.wait_ge(x_split, 4 * (g - 1) + 2)
                for t in range(BT):
                    ins = nc.tensor.transpose(xT[:, t * P:(t + 1) * P],
                                              gathered[:, g % GATHERS, t, :, :].rearrange("p a d -> p (a d)"), ident[:, :])
                ins.then_inc(transposed, 1)

            def project(G):
                g, k, u = groups[G]
                m = step_of(g)[1]
                if k == m:
                    pe.wait_ge(x_split, 4 * (g + 1))
                    pe.wait_ge(w_lo_ready, weights_of_step(g)[-1][1] + 1)
                    pe.wait_ge(split_zeroed, 1)
                s = claim(pe, slot["project", G])
                for odd in ([0] if k == m else [0, 1]):
                    a = 2 * (k - m - odd)
                    w = w_split[:, (2 * m + odd) % WSLOTS, a:a + 2, :].rearrange("p a e -> p (a e)")
                    nc.tensor.matmul(left[:, s, odd, :], w, x_hi[:, g % 2, odd, :], start=True, stop=False)
                    ins = nc.tensor.matmul(left[:, s, odd, :], w, x_lo[:, g % 2, odd, :], start=False, stop=True)
                ins.then_inc(projected, 1)

            def reduce(G):
                g, k, u = groups[G]
                h, m = step_of(g)
                if G == 0:
                    pe.wait_ge(windows_ready, 4)
                pe.wait_ge(multiplied, G + 1)
                told = 0
                for j in range(1 if k == m else 2):
                    v = u + j
                    q, t = v % 4, v % CHUNK // 4
                    if v % CHUNK == 0 and v:
                        pe.wait_ge(z_copied, v // CHUNK)
                    window = diag_window[:, m, :] if k == m else ones_window[:, :]
                    ins = nc.tensor.matmul(z_sum[32 * q:32 * q + 32, :], window[:, 30 - 2 * t:62 - 2 * t],
                                           diagonal[:, h, :] if k == m else products[:, G % PRODS, j, :],
                                           start=(t == 0), stop=(t == CHUNK // 4 - 1))
                    if v % CHUNK == CHUNK - 1 and v + 1 < units_through(G):
                        ins.then_inc(reduced, 1)
                        told += 1
                ins.then_inc(reduced, j + 1 - told)

            def layer(what, h):
                stationary, moving, chunks = {
                    "layer1": (w1_sb, z, CHUNKS), "layer2": (w2_sb, h1, H1 // P), "layer3": (w3_sb, h2, H2 // P)}[what]
                if what == "layer1":
                    pe.wait_ge(w1_loaded, 16 * CHUNKS)
                    pe.wait_ge(z_copied, CHUNKS * (h + 1))
                elif what == "layer2":
                    pe.wait_ge(mlp_loaded, 64)
                    pe.wait_ge(layer_copied, 4 * h + 2)
                else:
                    pe.wait_ge(layer_copied, 4 * h + 3)
                for piece in range(2 if what == "layer1" else 1):
                    s = claim(pe, slot[what, h, piece])
                    for j in range(1 if what == "layer3" else 2):
                        n = 2 * piece + j
                        for c in range(chunks):
                            if what == "layer3":
                                to, w = left[0:1, s, 0, :], w3_sb[:, c:c + 1]
                            else:
                                to, w = left[:, s, j, :], stationary[:, c, n * P:(n + 1) * P]
                            ins = nc.tensor.matmul(to, w, moving[:, c, :], start=(c == 0), stop=(c == chunks - 1))
                    ins.then_inc(layer_summed, 1)

            for what, n in plan:
                if what == "context":
                    transpose_context(n)
                elif what == "transpose":
                    transpose_x(n)
                elif what == "project":
                    project(n)
                elif what == "reduce":
                    reduce(n)
                elif what.startswith("layer"):
                    layer(what, n)


def kernel(**inputs):
    import concourse.bacc as _bacc
    from concourse.bass_utils import run_bass_kernel_spmd as _run

    nc = _bacc.Bacc("TRN2", target_bir_lowering=False, num_devices=1)
    arrays = {}

    def given(name, a):
        a = np.ascontiguousarray(a)
        arrays[f"in_{name}_dram"] = a
        return nc.dram_tensor(f"in_{name}_dram", a.shape, mybir.dt.from_np(a.dtype), kind="ExternalInput").ap()

    tables = [given(f"tbl_{f}", inputs[f"tbl_{f}"]) for f in range(F)]
    args = [given(n, inputs[n]) for n in ("L0_rec_W", "W_top1", "b_top1", "W_top2", "b_top2", "W_top3")]
    ctx_and_ids = [given(n, inputs[n]) for n in ("dense_ctx", "ids")]
    index = given("w1_rows", w1_rows())
    out = nc.dram_tensor("out_0_dram", (B, 1), F32, kind="ExternalOutput").ap()
    dlrm_tower(nc, *ctx_and_ids, tables, *args, index, out)
    r = _run(nc, [arrays], core_ids=[0])
    return r.results[0]["out_0_dram"]
```

```python
from contextlib import ExitStack

import numpy as np

import concourse.bass as bass
from concourse import mybir

ALU = mybir.AluOpType
ACT = mybir.ActivationFunctionType
F32 = mybir.dt.float32
F32R = mybir.dt.float32r

P = 128
B = 1024
F = 32
D = 64
FP = F // 2
HB = 512
HALVES = B // HB
BT = HB // P
NPAIR = F * (F - 1) // 2
NCTX = 16
STEPS = FP * HALVES

UNITS = 2 * NPAIR // 4 + FP // 2
CHUNK = 64
CHUNKS = UNITS // CHUNK
H1, H2 = 512, 256

RING = 3
REDUCE_LAG = 2
REDUCE_BATCH = 3
PRODS = REDUCE_LAG + REDUCE_BATCH
RAW = 2
WSLOTS = 4
GATHERS = 4
X_RING = 4
X_SLOTS = FP + 4
RESIDENT = 6
PIECE = 8
BUSY_GATHERING = 13
BUSY_AGAIN = 8


def first_pair(i):
    return sum(F - 1 - a for a in range(i))


def step_of(g):
    return g // FP, FP - 1 - g % FP


def resident(g):
    return g % FP < RESIDENT


def fields_to_split(g):
    h, m = step_of(g)
    return [i for i in (2 * m + 1, 2 * m) if i < F - 1 and not (h and resident(g))]


def pool_splits(g):
    return g % FP >= (BUSY_AGAIN if g >= FP else BUSY_GATHERING)


def pieces_of_field(i):
    pairs = F - 1 - i
    return [(a, min(PIECE, pairs - a)) for a in range(0, pairs, PIECE)]


def groups_of_step(m):
    return [m] + list(range(FP - 1, m, -1))


def row_fields():
    rows = []
    for g in range(FP):
        m = step_of(g)[1]
        for k in groups_of_step(m):
            if k == m:
                rows.append((NPAIR + m, first_pair(2 * m)))
            else:
                for i in (2 * m, 2 * m + 1):
                    a = first_pair(i) + 2 * k - i - 1
                    rows.append((a, a + 1))
    return rows


def z_row(u):
    return 32 * (u % 4) + 2 * (u % CHUNK // 4)


def w1_rows():
    index = np.zeros((P, CHUNKS), np.int32)
    for u, (a, b) in enumerate(row_fields()):
        index[z_row(u), u // CHUNK] = a
        index[z_row(u) + 1, u // CHUNK] = b
    return index


def make_plan():
    groups, pieces, prepare = [], [], []
    units = 0
    for g in range(STEPS):
        for k in groups_of_step(step_of(g)[1]):
            groups.append((g, k, units))
            units += 1 if k == step_of(g)[1] else 2
        mine = []
        for i in fields_to_split(g):
            for a, n in pieces_of_field(i):
                mine.append(("split_w", len(pieces)))
                pieces.append((g, i, a, n))
        prepare.append((mine, [("transpose", g), ("split_x", (g, 0)), ("split_x", (g, 1))]))
    first = [next(G for G, x in enumerate(groups) if x[0] == g) for g in range(STEPS)] + [len(groups)]

    before = [[] for _ in groups]
    rows = [(odd, t) for odd in (0, 1) for t in range(BT)]
    for g in range(STEPS):
        w, x = prepare[g]
        if g == 0:
            before[0] += [("gather", (a, *row)) for a in range(GATHERS + 1) for row in rows] + w + x
            continue
        begin, end = first[g - 1], first[g]
        if g > FP // 2:
            end -= 2
        if g <= FP:
            at = min(end, begin + 1)
        else:
            at = min(end, max(first[g - X_RING + 1], end - 16, at + 4))
        for n, piece in enumerate(w):
            spot = begin + n * (end - begin) // len(w)
            before[spot].append(piece)
        before[at] += x[:1]
        if g + GATHERS < STEPS:
            for n, row in enumerate(rows):
                before[at + (n + 1 if g + GATHERS > FP else 0)].append(("gather", (g + GATHERS, *row)))
            if g + GATHERS == FP:
                before[at].append(("gather_w1", 0))
        before[min(end, at + 3)] += x[1:2]
        before[min(end, at + 4)] += x[2:]

    plan, done, diagonal = [("context", h) for h in range(HALVES)], 0, -1

    def reduce_up_to(n):
        nonlocal done
        while done < n:
            plan.append(("reduce", done))
            done += 1

    for G, (g, k, u) in enumerate(groups):
        h, m = step_of(g)
        if k == m:
            reduce_up_to(diagonal + 1)
            diagonal = G
            if h and g % FP in (2, 3, 4):
                reduce_up_to(first[FP])
                plan.append((f"layer{g % FP - 1}", 0))
        plan += before[G]
        plan.append(("project", G))
        if G + 1 - done >= REDUCE_LAG + REDUCE_BATCH:
            reduce_up_to(done + REDUCE_BATCH)
    reduce_up_to(len(groups))
    plan += [(f"layer{n}", HALVES - 1) for n in (1, 2, 3)]
    return plan, groups, pieces


def dlrm_tower(nc, dense_ctx, ids, tables, W, W1, b1, W2, b2, W3, w1_index, out):
    plan, groups, pieces = make_plan()
    last_of_chunk = {}
    for G, (g, k, u) in enumerate(groups):
        n = 1 if k == step_of(g)[1] else 2
        for x in range(u, u + n):
            if x % CHUNK == CHUNK - 1:
                last_of_chunk[G] = x // CHUNK
    ctx = ExitStack()
    with ctx:
        def sb(name, shape, dt=F32):
            return ctx.enter_context(nc.sbuf_tensor(name, shape, dt))

        def sem(name):
            return ctx.enter_context(nc.semaphore(name))

        ids_sb = sb("ids_sb", [P, HALVES * BT, F], mybir.dt.int32)
        w1_index_sb = sb("w1_index_sb", [P, CHUNKS], mybir.dt.int32)
        context_rows = sb("context_rows", [P, HALVES * BT, NCTX])
        gathered = sb("gathered", [P, GATHERS, BT, 2, D])
        raw_w = sb("raw_w", [D, RAW, F - 1, D])
        w_split = sb("w_split", [P, WSLOTS, F, D], F32R)
        w_resident = sb("w_resident", [P, 2 * RESIDENT ** 2, D], F32R)
        x_hi = sb("x_hi", [P, X_RING, 2, HB], F32R)
        x_lo = sb("x_lo", [P, X_RING, 2, HB], F32R)
        X = sb("X", [P, X_SLOTS, HB])
        products = sb("products", [P, PRODS, 2, HB])
        diagonal = sb("diagonal", [P, HALVES, HB])
        ident = sb("ident", [P, P])
        ones_window = sb("ones_window", [P, 62])
        diag_window = sb("diag_window", [P, FP, 62])
        z = sb("z", [P, CHUNKS, HB])
        h1 = sb("h1", [P, H1 // P, HB])
        h2 = sb("h2", [P, H2 // P, HB])
        w1_sb = sb("w1_sb", [P, CHUNKS, H1])
        w2_sb = sb("w2_sb", [P, H1 // P, H2])
        w3_sb = sb("w3_sb", [P, H2 // P])
        b1_sb = sb("b1_sb", [P, H1 // P])
        b2_sb = sb("b2_sb", [P, H2 // P])
        y = h1[0:1, 0, :]

        left = ctx.enter_context(nc.psum_tensor("left", [P, RING, 2, HB], F32))
        xT = ctx.enter_context(nc.psum_tensor("xT", [P, HB], F32))
        z_sum = ctx.enter_context(nc.psum_tensor("z_sum", [P, HB], F32))

        ids_loaded = sem("ids_loaded")
        index_loaded = sem("index_loaded")
        context_loaded = sem("context_loaded")
        w1_loaded = sem("w1_loaded")
        mlp_loaded = sem("mlp_loaded")
        raw_loaded = [sem(f"raw_loaded{r}") for r in range(RAW)]
        rows_gathered = [sem(f"rows_gathered{r}") for r in range(GATHERS)]
        constants_zeroed = sem("constants_zeroed")
        ident_ready = sem("ident_ready")
        windows_ready = sem("windows_ready")
        diagonal_zeroed = sem("diagonal_zeroed")
        split_zeroed = sem("split_zeroed")
        transposed = sem("transposed")
        context_placed = sem("context_placed")
        x_hi_natural = sem("x_hi_natural")
        x_copied = sem("x_copied")
        x_lo_natural = sem("x_lo_natural")
        x_hi_doubled = sem("x_hi_doubled")
        x_lo_doubled = sem("x_lo_doubled")
        w_hi_ready = sem("w_hi_ready")
        w_lo_by_dve = sem("w_lo_by_dve")
        w_lo_by_pool = sem("w_lo_by_pool")
        projected = sem("projected")
        multiplied = sem("multiplied")
        reduced = sem("reduced")
        z_copied = sem("z_copied")
        layer_summed = sem("layer_summed")
        layer_copied = sem("layer_copied")
        y_stored = sem("y_stored")

        slot, freed, use, mlp_piece = {}, [], 0, 0
        for what, n in plan:
            if what == "project":
                slot[what, n] = use
                freed.append((multiplied, n + 1))
                use += 1
            elif what.startswith("layer"):
                for piece in range(2 if what == "layer1" else 1):
                    slot[what, n, piece] = use
                    mlp_piece += 1
                    freed.append((layer_copied, mlp_piece))
                    use += 1

        def claim(eng, n):
            if n >= RING:
                eng.wait_ge(*freed[n - RING])
            return n % RING

        def groups_through(g):
            return sum(1 for x in groups if x[0] <= g)

        diag_group = [next(G for G, x in enumerate(groups) if x[0] == g) for g in range(STEPS)]

        last_use = {}
        for G, (g, k, u) in enumerate(groups):
            last_use[step_of(g)[0], k] = G

        def units_through(G):
            g, k, u = groups[G]
            return u + (1 if k == step_of(g)[1] else 2)

        loads = [(g, i) for g in range(STEPS) for i in fields_to_split(g)]
        last_piece = {x[:2]: n for n, x in enumerate(pieces)}

        def weights(g, i, part, cell, n):
            s = g % FP
            if resident(g):
                at = 2 * (s * s + (s + 1) * (i % 2)) + cell
                return w_resident[part, at:at + n, :]
            return w_split[part, i % WSLOTS, cell:cell + n, :]

        def wait_w_lo(eng, n):
            by_pool = pool_splits(pieces[n][0])
            made = sum(1 for x in pieces[:n + 1] if pool_splits(x[0]) == by_pool)
            eng.wait_ge(w_lo_by_pool if by_pool else w_lo_by_dve, made)

        def x_slot(h, k):
            return (FP * h + FP - 1 - k) % X_SLOTS

        block = ctx.enter_context(nc.Block())

        def split_w_lo(eng, n, made):
            g, i, a, pairs = pieces[n]
            load = loads.index((g, i))
            eng.wait_ge(w_hi_ready, n + 1)
            cell = a + 1 - i % 2
            eng.tensor_tensor(weights(g, i, slice(D, P), cell, pairs), raw_w[:, load % RAW, a:a + pairs, :],
                              weights(g, i, slice(0, D), cell, pairs).bitcast(F32), ALU.subtract).then_inc(made, 1)

        @block.sync
        def _(sp):
            sp.dma_start(ids_sb[:, :, :], ids.rearrange("(t p) f -> p t f", p=P)).then_inc(ids_loaded, 16)
            sp.dma_start(context_rows[:, :, :], dense_ctx.rearrange("(t p) f -> p t f", p=P)).then_inc(context_loaded, 16)
            sp.dma_start(w1_index_sb[:, :], w1_index).then_inc(index_loaded, 16)
            for n, (g, i) in enumerate(loads):
                if n >= RAW:
                    wait_w_lo(sp, last_piece[loads[n - RAW]])
                a, pairs = first_pair(i), F - 1 - i
                sp.dma_start(raw_w[:, n % RAW, 0:pairs, :],
                             W[a:a + pairs].rearrange("p d e -> d p e")).then_inc(raw_loaded[n % RAW], 16)
                if n == 6:
                    sp.dma_start(w2_sb[:, :, :], W2.rearrange("(c p) n -> p c n", p=P)).then_inc(mlp_loaded, 16)
                    with nc.allow_non_contiguous_dma(reason="a few hundred words"):
                        sp.dma_start(w3_sb[:, :], W3.rearrange("(c p) n -> p (c n)", p=P)).then_inc(mlp_loaded, 16)
                        sp.dma_start(b1_sb[:, :], b1.rearrange("(c p) -> p c", p=P)).then_inc(mlp_loaded, 16)
                        sp.dma_start(b2_sb[:, :], b2.rearrange("(c p) -> p c", p=P)).then_inc(mlp_loaded, 16)
            for h in range(HALVES):
                sp.wait_ge(layer_copied, 4 * (h + 1))
                sp.dma_start(out[h * HB:(h + 1) * HB, :].rearrange("b o -> o b"), y).then_inc(y_stored, 16)
            sp.wait_ge(y_stored, 16 * HALVES)

        @block.gpsimd
        def _(pool):
            nc.gpsimd.memset(ident[:, :], 0.0).then_inc(constants_zeroed, 1)
            nc.gpsimd.memset(ones_window[:, :], 0.0).then_inc(constants_zeroed, 1)
            nc.gpsimd.memset(diag_window[:, :, :], 0.0).then_inc(constants_zeroed, 1)
            pool.wait_ge(constants_zeroed, 3)
            nc.gpsimd.affine_select(out=ident[:, :], in_=ident[:, :], compare_op=ALU.not_equal, fill=1.0, base=0,
                                    pattern=[[-1, P]], channel_multiplier=1).then_inc(ident_ready, 1)
            pool.wait_ge(ids_loaded, 16)
            def gather(g, odd, t):
                h, m = step_of(g)
                f = 2 * m + odd
                if g >= GATHERS and (odd, t) == (0, 0):
                    pool.wait_ge(transposed, HALVES + g - GATHERS + 1)
                pool.indirect_dma_start(
                    out=gathered[:, g % GATHERS, t, odd, :], out_offset=None, in_=tables[f],
                    in_offset=bass.IndirectOffsetOnAxis(ap=ids_sb[:, h * BT + t, f:f + 1], axis=0),
                ).then_inc(rows_gathered[g % GATHERS], 16)

            def gather_w1():
                pool.wait_ge(index_loaded, 16)
                for c in range(CHUNKS):
                    pool.indirect_dma_start(
                        out=w1_sb[:, c, :], out_offset=None, in_=W1,
                        in_offset=bass.IndirectOffsetOnAxis(ap=w1_index_sb[:, c:c + 1], axis=0),
                    ).then_inc(w1_loaded, 16)

            for what, n in plan:
                if what == "gather":
                    gather(*n)
                elif what == "gather_w1":
                    gather_w1()
                elif what == "split_w" and pool_splits(pieces[n][0]):
                    split_w_lo(pool, n, w_lo_by_pool)

        @block.vector
        def _(dve):
            nc.vector.memset(diagonal[:, :, :], 0.0).then_inc(diagonal_zeroed, 1)
            nc.vector.memset(w_split[:, 0:WSLOTS:2, 0, :].bitcast(F32), 0.0).then_inc(split_zeroed, 1)
            for g in range(RESIDENT):
                nc.vector.memset(weights(g, 2 * step_of(g)[1], slice(0, P), 0, 1).bitcast(F32), 0.0).then_inc(split_zeroed, 1)
            dve.wait_ge(constants_zeroed, 3)
            nc.vector.memset(ones_window[0:D, 30:31], 1.0).then_inc(windows_ready, 1)
            nc.vector.memset(ones_window[D:P, 31:32], 1.0).then_inc(windows_ready, 1)
            nc.vector.memset(diag_window[D:P, :, 31:32], 1.0).then_inc(windows_ready, 1)
            dve.wait_ge(ident_ready, 1)
            nc.vector.tensor_copy(diag_window[0:NCTX, :, 30], ident[0:NCTX, 0:FP]).then_inc(windows_ready, 1)

            def split_x(g, odd):
                dve.wait_ge(x_hi_natural, 2 * (g + 1))
                dve.wait_ge(x_copied, g + 1)
                h, m = step_of(g)
                if g >= X_RING:
                    dve.wait_ge(projected, groups_through(g - X_RING))
                at = slice(D * odd, D * odd + D)
                nc.vector.tensor_tensor(x_lo[at, g % X_RING, odd, :], X[at, x_slot(h, m), :],
                                        x_hi[at, g % X_RING, odd, :].bitcast(F32), ALU.subtract).then_inc(x_lo_natural, 1)

            def multiply(G):
                g, k, u = groups[G]
                h, m = step_of(g)
                s = slot["project", G] % RING
                dve.wait_ge(projected, G + 1)
                if k == m:
                    if g % FP == 0:
                        dve.wait_ge(context_placed, h + 1)
                    else:
                        dve.wait_ge(reduced, units_through(diag_group[g - 1]))
                    nc.vector.tensor_tensor(diagonal[D:P, h, :], left[D:P, s, 0, :], X[D:P, x_slot(h, k), :],
                                            ALU.mult).then_inc(multiplied, 1)
                    return
                if G >= PRODS:
                    dve.wait_ge(reduced, units_through(G - PRODS))
                nc.vector.tensor_tensor(products[:, G % PRODS, :, :], left[:, s, :, :],
                                        X[:, x_slot(h, k):x_slot(h, k) + 1, :].to_broadcast([P, 2, HB]), ALU.mult).then_inc(multiplied, 1)

            for what, n in plan:
                if what == "split_x":
                    split_x(*n)
                elif what == "split_w" and not pool_splits(pieces[n][0]):
                    split_w_lo(dve, n, w_lo_by_dve)
                elif what == "project":
                    multiply(n)

        @block.scalar
        def _(act):
            def place_context(h):
                act.wait_ge(transposed, h + 1)
                act.wait_ge(diagonal_zeroed, 1)
                nc.scalar.activation(diagonal[0:NCTX, h, :], xT[0:NCTX, :], ACT.Copy).then_inc(context_placed, 1)

            def read_transposed(g):
                h, m = step_of(g)
                act.wait_ge(transposed, HALVES + g + 1)
                if g >= X_RING:
                    act.wait_ge(projected, groups_through(g - X_RING))
                for odd in (0, 1):
                    at = slice(D * odd, D * odd + D)
                    nc.scalar.activation(x_hi[at, g % X_RING, odd, :], xT[at, :], ACT.Copy).then_inc(x_hi_natural, 1)
                if g >= X_SLOTS:
                    act.wait_ge(multiplied, last_use[step_of(g - X_SLOTS)] + 1)
                nc.scalar.activation(X[:, x_slot(h, m), :], xT[:, :], ACT.Copy).then_inc(x_copied, 1)
                for odd in (0, 1):
                    at, other = slice(D * odd, D * odd + D), slice(D - D * odd, P - D * odd)
                    nc.scalar.activation(x_hi[other, g % X_RING, odd, :], xT[at, :], ACT.Copy).then_inc(x_hi_doubled, 1)

            def double_lo(g, odd):
                act.wait_ge(x_lo_natural, 2 * g + odd + 1)
                at, other = slice(D * odd, D * odd + D), slice(D - D * odd, P - D * odd)
                nc.scalar.activation(x_lo[other, g % X_RING, odd, :], x_lo[at, g % X_RING, odd, :].bitcast(F32),
                                     ACT.Copy).then_inc(x_lo_doubled, 1)

            def round_w(n):
                g, i, a, pairs = pieces[n]
                load = loads.index((g, i))
                act.wait_ge(raw_loaded[load % RAW], 16 * (load // RAW + 1))
                if g >= 2:
                    act.wait_ge(projected, groups_through(g - 2))
                nc.scalar.activation(weights(g, i, slice(0, D), a + 1 - i % 2, pairs),
                                     raw_w[:, load % RAW, a:a + pairs, :], ACT.Copy).then_inc(w_hi_ready, 1)

            def copy_z(G):
                c = last_of_chunk[G]
                act.wait_ge(reduced, CHUNK * (c + 1))
                if c >= CHUNKS:
                    act.wait_ge(layer_summed, 4 * (c // CHUNKS - 1) + 2)
                nc.scalar.activation(z[:, c % CHUNKS, :], z_sum[:, :], ACT.Copy).then_inc(z_copied, 1)

            def relu(what, h, piece):
                s = slot[what, h, piece] % RING
                n = 4 * h + {"layer1": 0, "layer2": 2}[what] + piece
                act.wait_ge(layer_summed, n + 1)
                act.wait_ge(mlp_loaded, 64)
                if what == "layer1" and h:
                    act.wait_ge(y_stored, 16 * h)
                for j in (0, 1):
                    c = 2 * piece + j
                    to, bias = (h1, b1_sb) if what == "layer1" else (h2, b2_sb)
                    ins = nc.scalar.activation(to[:, c, :], left[:, s, j, :], ACT.Relu, bias=bias[:, c:c + 1])
                ins.then_inc(layer_copied, 1)

            for what, n in plan:
                if what == "context":
                    place_context(n)
                elif what == "transpose":
                    read_transposed(n)
                elif what == "split_x":
                    double_lo(*n)
                elif what == "split_w":
                    round_w(n)
                elif what == "reduce" and n in last_of_chunk:
                    copy_z(n)
                elif what in ("layer1", "layer2"):
                    for piece in range(2 if what == "layer1" else 1):
                        relu(what, n, piece)
                elif what == "layer3":
                    act.wait_ge(layer_summed, 4 * n + 4)
                    nc.scalar.activation(y, left[0:1, slot[what, n, 0] % RING, 0, :],
                                         ACT.Copy).then_inc(layer_copied, 1)

        @block.tensor
        def _(pe):
            def transpose_context(h):
                if h == 0:
                    pe.wait_ge(ident_ready, 1)
                    pe.wait_ge(context_loaded, 16)
                else:
                    pe.wait_ge(context_placed, h)
                for t in range(BT):
                    ins = nc.tensor.transpose(xT[0:NCTX, t * P:(t + 1) * P], context_rows[:, h * BT + t, :], ident[:, :])
                ins.then_inc(transposed, 1)

            def transpose_x(g):
                pe.wait_ge(rows_gathered[g % GATHERS], 16 * 2 * BT * (g // GATHERS + 1))
                if g == 0:
                    pe.wait_ge(context_placed, HALVES)
                else:
                    pe.wait_ge(x_hi_doubled, 2 * g)
                for t in range(BT):
                    ins = nc.tensor.transpose(xT[:, t * P:(t + 1) * P],
                                              gathered[:, g % GATHERS, t, :, :].rearrange("p a d -> p (a d)"), ident[:, :])
                ins.then_inc(transposed, 1)

            def project(G):
                g, k, u = groups[G]
                m = step_of(g)[1]
                if k == m:
                    pe.wait_ge(x_hi_doubled, 2 * (g + 1))
                    pe.wait_ge(x_lo_doubled, 2 * (g + 1))
                    if fields_to_split(g):
                        wait_w_lo(pe, last_piece[g, 2 * m])
                    pe.wait_ge(split_zeroed, 1 + RESIDENT)
                s = claim(pe, slot["project", G])
                for odd in ([0] if k == m else [0, 1]):
                    w = weights(g, 2 * m + odd, slice(0, P), 2 * (k - m - odd), 2).rearrange("p a e -> p (a e)")
                    nc.tensor.matmul(left[:, s, odd, :], w, x_hi[:, g % X_RING, odd, :], start=True, stop=False)
                    ins = nc.tensor.matmul(left[:, s, odd, :], w, x_lo[:, g % X_RING, odd, :], start=False, stop=True)
                ins.then_inc(projected, 1)

            def reduce(G):
                g, k, u = groups[G]
                h, m = step_of(g)
                if G == 0:
                    pe.wait_ge(windows_ready, 4)
                pe.wait_ge(multiplied, G + 1)
                told = 0
                for j in range(1 if k == m else 2):
                    v = u + j
                    q, t = v % 4, v % CHUNK // 4
                    if v % CHUNK == 0 and v:
                        pe.wait_ge(z_copied, v // CHUNK)
                    window = diag_window[:, m, :] if k == m else ones_window[:, :]
                    ins = nc.tensor.matmul(z_sum[32 * q:32 * q + 32, :], window[:, 30 - 2 * t:62 - 2 * t],
                                           diagonal[:, h, :] if k == m else products[:, G % PRODS, j, :],
                                           start=(t == 0), stop=(t == CHUNK // 4 - 1))
                    if v % CHUNK == CHUNK - 1 and v + 1 < units_through(G):
                        ins.then_inc(reduced, 1)
                        told += 1
                ins.then_inc(reduced, j + 1 - told)

            def layer(what, h):
                stationary, moving, chunks = {
                    "layer1": (w1_sb, z, CHUNKS), "layer2": (w2_sb, h1, H1 // P), "layer3": (w3_sb, h2, H2 // P)}[what]
                if what == "layer1":
                    pe.wait_ge(w1_loaded, 16 * CHUNKS)
                    pe.wait_ge(z_copied, CHUNKS * (h + 1))
                elif what == "layer2":
                    pe.wait_ge(mlp_loaded, 64)
                    pe.wait_ge(layer_copied, 4 * h + 2)
                else:
                    pe.wait_ge(layer_copied, 4 * h + 3)
                for piece in range(2 if what == "layer1" else 1):
                    s = claim(pe, slot[what, h, piece])
                    for j in range(1 if what == "layer3" else 2):
                        n = 2 * piece + j
                        for c in range(chunks):
                            if what == "layer3":
                                to, w = left[0:1, s, 0, :], w3_sb[:, c:c + 1]
                            else:
                                to, w = left[:, s, j, :], stationary[:, c, n * P:(n + 1) * P]
                            ins = nc.tensor.matmul(to, w, moving[:, c, :], start=(c == 0), stop=(c == chunks - 1))
                    ins.then_inc(layer_summed, 1)

            for what, n in plan:
                if what == "context":
                    transpose_context(n)
                elif what == "transpose":
                    transpose_x(n)
                elif what == "project":
                    project(n)
                elif what == "reduce":
                    reduce(n)
                elif what.startswith("layer"):
                    layer(what, n)


def kernel(**inputs):
    import concourse.bacc as _bacc
    from concourse.bass_utils import run_bass_kernel_spmd as _run

    nc = _bacc.Bacc("TRN2", target_bir_lowering=False, num_devices=1)
    arrays = {}

    def given(name, a):
        a = np.ascontiguousarray(a)
        arrays[f"in_{name}_dram"] = a
        return nc.dram_tensor(f"in_{name}_dram", a.shape, mybir.dt.from_np(a.dtype), kind="ExternalInput").ap()

    tables = [given(f"tbl_{f}", inputs[f"tbl_{f}"]) for f in range(F)]
    args = [given(n, inputs[n]) for n in ("L0_rec_W", "W_top1", "b_top1", "W_top2", "b_top2", "W_top3")]
    ctx_and_ids = [given(n, inputs[n]) for n in ("dense_ctx", "ids")]
    index = given("w1_rows", w1_rows())
    out = nc.dram_tensor("out_0_dram", (B, 1), F32, kind="ExternalOutput").ap()
    dlrm_tower(nc, *ctx_and_ids, tables, *args, index, out)
    r = _run(nc, [arrays], core_ids=[0])
    return r.results[0]["out_0_dram"]
```

```python
from contextlib import ExitStack

import numpy as np

import concourse.bass as bass
from concourse import mybir

ALU = mybir.AluOpType
ACT = mybir.ActivationFunctionType
F32 = mybir.dt.float32
F32R = mybir.dt.float32r

P = 128
B = 1024
F = 32
D = 64
FP = F // 2
HB = 512
HALVES = B // HB
BT = HB // P
NPAIR = F * (F - 1) // 2
NCTX = 16
STEPS = FP * HALVES

UNITS = 2 * NPAIR // 4 + FP // 2
CHUNK = 64
CHUNKS = UNITS // CHUNK
H1, H2 = 512, 256
MLP_BANKS = H1 // P + H2 // P + 1

RING = 3
REDUCE_LAG = 2
REDUCE_BATCH = 3
PRODS = REDUCE_LAG + REDUCE_BATCH
RAW = 2
WSLOTS = 4
GATHERS = 4
X_RING = 4
X_SLOTS = 20
RESIDENT = 6
PIECE = 8

SHARED = (13, 7)
FREE = (13, 9)
DVE_PIECES = 1

X_LATEST = 11
X_AHEAD = 6
X_APART = 4
LO_AFTER = (1, 3)
ROWS_AFTER = 2
ROWS_AT_ONCE = FP + 4
MLP_STEPS = (2, 3, 4)


def first_pair(i):
    return sum(F - 1 - a for a in range(i))


def step_of(g):
    return g // FP, FP - 1 - g % FP


def resident(g):
    return g % FP < RESIDENT


def fields_to_split(g):
    h, m = step_of(g)
    return [i for i in (2 * m + 1, 2 * m) if i < F - 1 and not (h and resident(g))]


def pool_splits(piece):
    g, i, a, n = piece
    h, s = divmod(g, FP)
    return s >= FREE[h] or (s >= SHARED[h] and a >= DVE_PIECES * PIECE)


def pieces_of_field(i):
    pairs = F - 1 - i
    return [(a, min(PIECE, pairs - a)) for a in range(0, pairs, PIECE)]


def groups_of_step(m):
    return [m] + list(range(FP - 1, m, -1))


def row_fields():
    rows = []
    for g in range(FP):
        m = step_of(g)[1]
        for k in groups_of_step(m):
            if k == m:
                rows.append((NPAIR + m, first_pair(2 * m)))
            else:
                for i in (2 * m, 2 * m + 1):
                    a = first_pair(i) + 2 * k - i - 1
                    rows.append((a, a + 1))
    return rows


def z_row(u):
    return 32 * (u % 4) + 2 * (u % CHUNK // 4)


def w1_rows():
    index = np.zeros((P, CHUNKS), np.int32)
    for u, (a, b) in enumerate(row_fields()):
        index[z_row(u), u // CHUNK] = a
        index[z_row(u) + 1, u // CHUNK] = b
    return index


def make_plan():
    groups, pieces, prepare = [], [], []
    units = 0
    for g in range(STEPS):
        for k in groups_of_step(step_of(g)[1]):
            groups.append((g, k, units))
            units += 1 if k == step_of(g)[1] else 2
        mine = []
        for i in fields_to_split(g):
            for a, n in pieces_of_field(i):
                mine.append(("split_w", len(pieces)))
                pieces.append((g, i, a, n))
        prepare.append((mine, [("transpose", g), ("split_x", (g, 0)), ("split_x", (g, 1))]))
    first = [next(G for G, x in enumerate(groups) if x[0] == g) for g in range(STEPS)] + [len(groups)]

    before = [[] for _ in groups]
    rows = [(odd, t) for odd in (0, 1) for t in range(BT)]
    for g in range(STEPS):
        w, x = prepare[g]
        if g == 0:
            before[0] += [("gather", (a, *row)) for a in range(GATHERS + 1) for row in rows] + w + x
            continue
        begin, end = first[g - 1], first[g]
        if g > FP // 2:
            end -= 2
        if g <= FP:
            rows_at = min(end, begin + 1)
            at = max(rows_at, end - X_LATEST)
        else:
            at = rows_at = min(end, max(first[g - X_RING + 1], end - X_AHEAD, at + X_APART))
        for n, piece in enumerate(w):
            before[begin + n * (end - begin) // len(w)].append(piece)
        before[at] += x[:1]
        if g + GATHERS < STEPS:
            for n, row in enumerate(rows):
                spot = rows_at + (ROWS_AFTER + n if g + GATHERS > ROWS_AT_ONCE else 0)
                before[spot].append(("gather", (g + GATHERS, *row)))
            if g + GATHERS == FP:
                before[rows_at].append(("gather_w1", 0))
        for late, split in zip(LO_AFTER, x[1:]):
            before[min(end, at + late)].append(split)

    plan, done, diagonal = [("context", h) for h in range(HALVES)], 0, -1

    def reduce_up_to(n):
        nonlocal done
        while done < n:
            plan.append(("reduce", done))
            done += 1

    for G, (g, k, u) in enumerate(groups):
        h, m = step_of(g)
        if k == m:
            reduce_up_to(diagonal + 1)
            diagonal = G
            if h and g % FP in MLP_STEPS:
                reduce_up_to(first[FP])
                n = MLP_STEPS.index(g % FP) + 1
                plan += [("layer1_early", 0)] * (n == 1) + [(f"layer{n}", 0)]
        plan += before[G]
        plan.append(("project", G))
        if G + 1 - done >= REDUCE_LAG + REDUCE_BATCH:
            reduce_up_to(done + REDUCE_BATCH)
    plan.append(("layer1_early", HALVES - 1))
    reduce_up_to(len(groups))
    plan += [(f"layer{n}", HALVES - 1) for n in (1, 2, 3)]
    return plan, groups, pieces


def dlrm_tower(nc, dense_ctx, ids, tables, W, W1, b1, W2, b2, W3, w1_index, out):
    plan, groups, pieces = make_plan()
    last_of_chunk = {}
    for G, (g, k, u) in enumerate(groups):
        n = 1 if k == step_of(g)[1] else 2
        for x in range(u, u + n):
            if x % CHUNK == CHUNK - 1:
                last_of_chunk[G] = x // CHUNK
    ctx = ExitStack()
    with ctx:
        def sb(name, shape, dt=F32):
            return ctx.enter_context(nc.sbuf_tensor(name, shape, dt))

        def sem(name):
            return ctx.enter_context(nc.semaphore(name))

        ids_sb = sb("ids_sb", [P, HALVES * BT, F], mybir.dt.int32)
        w1_index_sb = sb("w1_index_sb", [P, CHUNKS], mybir.dt.int32)
        context_rows = sb("context_rows", [P, HALVES * BT, NCTX])
        gathered = sb("gathered", [P, GATHERS, BT, 2, D])
        raw_w = sb("raw_w", [D, RAW, F - 1, D])
        w_split = sb("w_split", [P, WSLOTS, F, D], F32R)
        w_resident = sb("w_resident", [P, 2 * RESIDENT ** 2, D], F32R)
        x_hi = sb("x_hi", [P, X_RING, 2, HB], F32R)
        x_lo = sb("x_lo", [P, X_RING, 2, HB], F32R)
        X = sb("X", [P, X_SLOTS, HB])
        products = sb("products", [P, PRODS, 2, HB])
        diagonal = sb("diagonal", [P, HALVES, HB])
        ident = sb("ident", [P, P])
        ones_window = sb("ones_window", [P, 62])
        diag_window = sb("diag_window", [P, FP, 62])
        z = sb("z", [P, CHUNKS, HB])
        h1 = sb("h1", [P, H1 // P, HB])
        h2 = sb("h2", [P, H2 // P, HB])
        w1_sb = sb("w1_sb", [P, CHUNKS, H1])
        w2_sb = sb("w2_sb", [P, H1 // P, H2])
        w3_sb = sb("w3_sb", [P, H2 // P])
        b1_sb = sb("b1_sb", [P, H1 // P])
        b2_sb = sb("b2_sb", [P, H2 // P])
        y = h1[0:1, 0, :]

        left = ctx.enter_context(nc.psum_tensor("left", [P, RING, 2, HB], F32))
        xT = ctx.enter_context(nc.psum_tensor("xT", [P, HB], F32))
        z_sum = ctx.enter_context(nc.psum_tensor("z_sum", [P, HB], F32))

        ids_loaded = sem("ids_loaded")
        index_loaded = sem("index_loaded")
        context_loaded = sem("context_loaded")
        w1_loaded = sem("w1_loaded")
        mlp_loaded = sem("mlp_loaded")
        raw_loaded = [sem(f"raw_loaded{r}") for r in range(RAW)]
        rows_gathered = [sem(f"rows_gathered{r}") for r in range(GATHERS)]
        constants_zeroed = sem("constants_zeroed")
        ident_ready = sem("ident_ready")
        windows_ready = sem("windows_ready")
        diagonal_zeroed = sem("diagonal_zeroed")
        split_zeroed = sem("split_zeroed")
        transposed = sem("transposed")
        context_placed = sem("context_placed")
        x_hi_natural = sem("x_hi_natural")
        x_copied = sem("x_copied")
        x_lo_natural = sem("x_lo_natural")
        x_hi_doubled = sem("x_hi_doubled")
        x_lo_doubled = sem("x_lo_doubled")
        w_hi_ready = sem("w_hi_ready")
        w_lo_by_dve = sem("w_lo_by_dve")
        w_lo_by_pool = sem("w_lo_by_pool")
        projected = sem("projected")
        multiplied = sem("multiplied")
        reduced = sem("reduced")
        z_copied = sem("z_copied")
        layer_summed = sem("layer_summed")
        layer_copied = sem("layer_copied")
        y_stored = sem("y_stored")

        slot, freed, use, mlp_banks = {}, [], 0, 0
        for what, n in plan:
            if what == "project":
                slot[what, n] = use
                freed.append((multiplied, n + 1))
                use += 1
            elif what in ("layer1_early", "layer2", "layer3"):
                for piece in range(2 if what == "layer1_early" else 1):
                    slot[what.removesuffix("_early"), n, piece] = use
                    mlp_banks += 1 if what == "layer3" else 2
                    freed.append((layer_copied, mlp_banks))
                    use += 1

        def claim(eng, n):
            if n >= RING:
                eng.wait_ge(*freed[n - RING])
            return n % RING

        def groups_through(g):
            return sum(1 for x in groups if x[0] <= g)

        diag_group = [next(G for G, x in enumerate(groups) if x[0] == g) for g in range(STEPS)]

        last_use = {}
        for G, (g, k, u) in enumerate(groups):
            last_use[step_of(g)[0], k] = G

        def units_through(G):
            g, k, u = groups[G]
            return u + (1 if k == step_of(g)[1] else 2)

        loads = [(g, i) for g in range(STEPS) for i in fields_to_split(g)]
        last_piece = {x[:2]: n for n, x in enumerate(pieces)}

        def weights(g, i, part, cell, n):
            s = g % FP
            if resident(g):
                at = 2 * (s * s + (s + 1) * (i % 2)) + cell
                return w_resident[part, at:at + n, :]
            return w_split[part, i % WSLOTS, cell:cell + n, :]

        def wait_w_lo(eng, n):
            by_pool = sum(pool_splits(x) for x in pieces[:n + 1])
            by_dve = n + 1 - by_pool
            if by_pool:
                eng.wait_ge(w_lo_by_pool, by_pool)
            if by_dve:
                eng.wait_ge(w_lo_by_dve, by_dve)

        def x_slot(h, k):
            return (FP * h + FP - 1 - k) % X_SLOTS

        block = ctx.enter_context(nc.Block())

        def split_w_lo(eng, n, made):
            g, i, a, pairs = pieces[n]
            load = loads.index((g, i))
            eng.wait_ge(w_hi_ready, n + 1)
            cell = a + 1 - i % 2
            eng.tensor_tensor(weights(g, i, slice(D, P), cell, pairs), raw_w[:, load % RAW, a:a + pairs, :],
                              weights(g, i, slice(0, D), cell, pairs).bitcast(F32), ALU.subtract).then_inc(made, 1)

        @block.sync
        def _(sp):
            sp.dma_start(ids_sb[:, :, :], ids.rearrange("(t p) f -> p t f", p=P)).then_inc(ids_loaded, 16)
            sp.dma_start(context_rows[:, :, :], dense_ctx.rearrange("(t p) f -> p t f", p=P)).then_inc(context_loaded, 16)
            sp.dma_start(w1_index_sb[:, :], w1_index).then_inc(index_loaded, 16)
            for n, (g, i) in enumerate(loads):
                if n >= RAW:
                    wait_w_lo(sp, last_piece[loads[n - RAW]])
                a, pairs = first_pair(i), F - 1 - i
                sp.dma_start(raw_w[:, n % RAW, 0:pairs, :],
                             W[a:a + pairs].rearrange("p d e -> d p e")).then_inc(raw_loaded[n % RAW], 16)
                if n == 6:
                    sp.dma_start(w2_sb[:, :, :], W2.rearrange("(c p) n -> p c n", p=P)).then_inc(mlp_loaded, 16)
                    with nc.allow_non_contiguous_dma(reason="a few hundred words"):
                        sp.dma_start(w3_sb[:, :], W3.rearrange("(c p) n -> p (c n)", p=P)).then_inc(mlp_loaded, 16)
                        sp.dma_start(b1_sb[:, :], b1.rearrange("(c p) -> p c", p=P)).then_inc(mlp_loaded, 16)
                        sp.dma_start(b2_sb[:, :], b2.rearrange("(c p) -> p c", p=P)).then_inc(mlp_loaded, 16)
            for h in range(HALVES):
                sp.wait_ge(layer_copied, MLP_BANKS * (h + 1))
                sp.dma_start(out[h * HB:(h + 1) * HB, :].rearrange("b o -> o b"), y).then_inc(y_stored, 16)
            sp.wait_ge(y_stored, 16 * HALVES)

        @block.gpsimd
        def _(pool):
            nc.gpsimd.memset(ident[:, :], 0.0).then_inc(constants_zeroed, 1)
            nc.gpsimd.memset(ones_window[:, :], 0.0).then_inc(constants_zeroed, 1)
            nc.gpsimd.memset(diag_window[:, :, :], 0.0).then_inc(constants_zeroed, 1)
            pool.wait_ge(constants_zeroed, 3)
            nc.gpsimd.affine_select(out=ident[:, :], in_=ident[:, :], compare_op=ALU.not_equal, fill=1.0, base=0,
                                    pattern=[[-1, P]], channel_multiplier=1).then_inc(ident_ready, 1)
            pool.wait_ge(ids_loaded, 16)
            def gather(g, odd, t):
                h, m = step_of(g)
                f = 2 * m + odd
                if g >= GATHERS and (odd, t) == (0, 0):
                    pool.wait_ge(transposed, HALVES + g - GATHERS + 1)
                pool.indirect_dma_start(
                    out=gathered[:, g % GATHERS, t, odd, :], out_offset=None, in_=tables[f],
                    in_offset=bass.IndirectOffsetOnAxis(ap=ids_sb[:, h * BT + t, f:f + 1], axis=0),
                ).then_inc(rows_gathered[g % GATHERS], 16)

            def gather_w1():
                pool.wait_ge(index_loaded, 16)
                for c in range(CHUNKS):
                    pool.indirect_dma_start(
                        out=w1_sb[:, c, :], out_offset=None, in_=W1,
                        in_offset=bass.IndirectOffsetOnAxis(ap=w1_index_sb[:, c:c + 1], axis=0),
                    ).then_inc(w1_loaded, 16)

            for what, n in plan:
                if what == "gather":
                    gather(*n)
                elif what == "gather_w1":
                    gather_w1()
                elif what == "split_w" and pool_splits(pieces[n]):
                    split_w_lo(pool, n, w_lo_by_pool)

        @block.vector
        def _(dve):
            nc.vector.memset(diagonal[:, :, :], 0.0).then_inc(diagonal_zeroed, 1)
            nc.vector.memset(w_split[:, 0:WSLOTS:2, 0, :].bitcast(F32), 0.0).then_inc(split_zeroed, 1)
            for g in range(RESIDENT):
                zeros = weights(g, 2 * step_of(g)[1], slice(0, P), 0, 1)
                nc.vector.memset(zeros.bitcast(F32), 0.0).then_inc(split_zeroed, 1)
            dve.wait_ge(constants_zeroed, 3)
            nc.vector.memset(ones_window[0:D, 30:31], 1.0).then_inc(windows_ready, 1)
            nc.vector.memset(ones_window[D:P, 31:32], 1.0).then_inc(windows_ready, 1)
            nc.vector.memset(diag_window[D:P, :, 31:32], 1.0).then_inc(windows_ready, 1)
            dve.wait_ge(ident_ready, 1)
            nc.vector.tensor_copy(diag_window[0:NCTX, :, 30], ident[0:NCTX, 0:FP]).then_inc(windows_ready, 1)

            def split_x(g, odd):
                dve.wait_ge(x_hi_natural, 2 * (g + 1))
                dve.wait_ge(x_copied, g + 1)
                h, m = step_of(g)
                if g >= X_RING:
                    dve.wait_ge(projected, groups_through(g - X_RING))
                at = slice(D * odd, D * odd + D)
                nc.vector.tensor_tensor(x_lo[at, g % X_RING, odd, :], X[at, x_slot(h, m), :],
                                        x_hi[at, g % X_RING, odd, :].bitcast(F32),
                                        ALU.subtract).then_inc(x_lo_natural, 1)

            def multiply(G):
                g, k, u = groups[G]
                h, m = step_of(g)
                s = slot["project", G] % RING
                dve.wait_ge(projected, G + 1)
                if k == m:
                    if g % FP == 0:
                        dve.wait_ge(context_placed, h + 1)
                    else:
                        dve.wait_ge(reduced, units_through(diag_group[g - 1]))
                    nc.vector.tensor_tensor(diagonal[D:P, h, :], left[D:P, s, 0, :], X[D:P, x_slot(h, k), :],
                                            ALU.mult).then_inc(multiplied, 1)
                    return
                if G >= PRODS:
                    dve.wait_ge(reduced, units_through(G - PRODS))
                nc.vector.tensor_tensor(products[:, G % PRODS, :, :], left[:, s, :, :],
                                        X[:, x_slot(h, k):x_slot(h, k) + 1, :].to_broadcast([P, 2, HB]),
                                        ALU.mult).then_inc(multiplied, 1)

            for what, n in plan:
                if what == "split_x":
                    split_x(*n)
                elif what == "split_w" and not pool_splits(pieces[n]):
                    split_w_lo(dve, n, w_lo_by_dve)
                elif what == "project":
                    multiply(n)

        @block.scalar
        def _(act):
            def place_context(h):
                act.wait_ge(transposed, h + 1)
                act.wait_ge(diagonal_zeroed, 1)
                nc.scalar.activation(diagonal[0:NCTX, h, :], xT[0:NCTX, :], ACT.Copy).then_inc(context_placed, 1)

            def read_transposed(g):
                h, m = step_of(g)
                act.wait_ge(transposed, HALVES + g + 1)
                if g >= X_RING:
                    act.wait_ge(projected, groups_through(g - X_RING))
                for odd in (0, 1):
                    at = slice(D * odd, D * odd + D)
                    nc.scalar.activation(x_hi[at, g % X_RING, odd, :], xT[at, :], ACT.Copy).then_inc(x_hi_natural, 1)
                if g >= X_SLOTS:
                    act.wait_ge(multiplied, last_use[step_of(g - X_SLOTS)] + 1)
                nc.scalar.activation(X[:, x_slot(h, m), :], xT[:, :], ACT.Copy).then_inc(x_copied, 1)
                for odd in (0, 1):
                    at, other = slice(D * odd, D * odd + D), slice(D - D * odd, P - D * odd)
                    nc.scalar.activation(x_hi[other, g % X_RING, odd, :], xT[at, :], ACT.Copy).then_inc(x_hi_doubled, 1)

            def double_lo(g, odd):
                act.wait_ge(x_lo_natural, 2 * g + odd + 1)
                at, other = slice(D * odd, D * odd + D), slice(D - D * odd, P - D * odd)
                nc.scalar.activation(x_lo[other, g % X_RING, odd, :], x_lo[at, g % X_RING, odd, :].bitcast(F32),
                                     ACT.Copy).then_inc(x_lo_doubled, 1)

            def round_w(n):
                g, i, a, pairs = pieces[n]
                load = loads.index((g, i))
                act.wait_ge(raw_loaded[load % RAW], 16 * (load // RAW + 1))
                if g >= 2:
                    act.wait_ge(projected, groups_through(g - 2))
                nc.scalar.activation(weights(g, i, slice(0, D), a + 1 - i % 2, pairs),
                                     raw_w[:, load % RAW, a:a + pairs, :], ACT.Copy).then_inc(w_hi_ready, 1)

            def copy_z(G):
                c = last_of_chunk[G]
                act.wait_ge(reduced, CHUNK * (c + 1))
                if c >= CHUNKS:
                    act.wait_ge(layer_summed, MLP_BANKS * (c // CHUNKS - 1) + H1 // P)
                nc.scalar.activation(z[:, c % CHUNKS, :], z_sum[:, :], ACT.Copy).then_inc(z_copied, 1)

            def relu(what, h, piece):
                s = slot[what, h, piece] % RING
                n = MLP_BANKS * h + {"layer1": 0, "layer2": H1 // P}[what] + 2 * piece
                act.wait_ge(mlp_loaded, 64)
                if what == "layer1" and h:
                    act.wait_ge(y_stored, 16 * h)
                for j in (0, 1):
                    c = 2 * piece + j
                    to, bias = (h1, b1_sb) if what == "layer1" else (h2, b2_sb)
                    act.wait_ge(layer_summed, n + j + 1)
                    nc.scalar.activation(to[:, c, :], left[:, s, j, :], ACT.Relu,
                                         bias=bias[:, c:c + 1]).then_inc(layer_copied, 1)

            for what, n in plan:
                if what == "context":
                    place_context(n)
                elif what == "transpose":
                    read_transposed(n)
                elif what == "split_x":
                    double_lo(*n)
                elif what == "split_w":
                    round_w(n)
                elif what == "reduce" and n in last_of_chunk:
                    copy_z(n)
                elif what in ("layer1", "layer2"):
                    for piece in range(2 if what == "layer1" else 1):
                        relu(what, n, piece)
                elif what == "layer3":
                    act.wait_ge(layer_summed, MLP_BANKS * (n + 1))
                    nc.scalar.activation(y, left[0:1, slot[what, n, 0] % RING, 0, :],
                                         ACT.Copy).then_inc(layer_copied, 1)

        @block.tensor
        def _(pe):
            def transpose_context(h):
                if h == 0:
                    pe.wait_ge(ident_ready, 1)
                    pe.wait_ge(context_loaded, 16)
                else:
                    pe.wait_ge(context_placed, h)
                for t in range(BT):
                    ins = nc.tensor.transpose(xT[0:NCTX, t * P:(t + 1) * P], context_rows[:, h * BT + t, :], ident[:, :])
                ins.then_inc(transposed, 1)

            def transpose_x(g):
                pe.wait_ge(rows_gathered[g % GATHERS], 16 * 2 * BT * (g // GATHERS + 1))
                if g == 0:
                    pe.wait_ge(context_placed, HALVES)
                else:
                    pe.wait_ge(x_hi_doubled, 2 * g)
                for t in range(BT):
                    ins = nc.tensor.transpose(xT[:, t * P:(t + 1) * P],
                                              gathered[:, g % GATHERS, t, :, :].rearrange("p a d -> p (a d)"), ident[:, :])
                ins.then_inc(transposed, 1)

            def project(G):
                g, k, u = groups[G]
                m = step_of(g)[1]
                if k == m:
                    pe.wait_ge(x_hi_doubled, 2 * (g + 1))
                    pe.wait_ge(x_lo_doubled, 2 * (g + 1))
                    if fields_to_split(g):
                        wait_w_lo(pe, last_piece[g, 2 * m])
                    pe.wait_ge(split_zeroed, 1 + RESIDENT)
                s = claim(pe, slot["project", G])
                for odd in ([0] if k == m else [0, 1]):
                    w = weights(g, 2 * m + odd, slice(0, P), 2 * (k - m - odd), 2).rearrange("p a e -> p (a e)")
                    nc.tensor.matmul(left[:, s, odd, :], w, x_hi[:, g % X_RING, odd, :], start=True, stop=False)
                    ins = nc.tensor.matmul(left[:, s, odd, :], w, x_lo[:, g % X_RING, odd, :], start=False, stop=True)
                ins.then_inc(projected, 1)

            def reduce(G):
                g, k, u = groups[G]
                h, m = step_of(g)
                if G == 0:
                    pe.wait_ge(windows_ready, 4)
                pe.wait_ge(multiplied, G + 1)
                told = 0
                for j in range(1 if k == m else 2):
                    v = u + j
                    q, t = v % 4, v % CHUNK // 4
                    if v % CHUNK == 0 and v:
                        pe.wait_ge(z_copied, v // CHUNK)
                    window = diag_window[:, m, :] if k == m else ones_window[:, :]
                    ins = nc.tensor.matmul(z_sum[32 * q:32 * q + 32, :], window[:, 30 - 2 * t:62 - 2 * t],
                                           diagonal[:, h, :] if k == m else products[:, G % PRODS, j, :],
                                           start=(t == 0), stop=(t == CHUNK // 4 - 1))
                    if v % CHUNK == CHUNK - 1 and v + 1 < units_through(G):
                        ins.then_inc(reduced, 1)
                        told += 1
                ins.then_inc(reduced, j + 1 - told)

            def layer1(h, early):
                pe.wait_ge(w1_loaded, 16 * CHUNKS)
                pe.wait_ge(z_copied, CHUNKS * (h + 1) - early)
                for piece in (0, 1):
                    s = claim(pe, slot["layer1", h, piece]) if early else slot["layer1", h, piece] % RING
                    for j in (0, 1):
                        n = 2 * piece + j
                        for c in range(CHUNKS - 1) if early else [CHUNKS - 1]:
                            ins = nc.tensor.matmul(left[:, s, j, :], w1_sb[:, c, n * P:(n + 1) * P], z[:, c, :],
                                                   start=(c == 0), stop=(c == CHUNKS - 1))
                        if not early:
                            ins.then_inc(layer_summed, 1)

            def layer2(h):
                pe.wait_ge(mlp_loaded, 64)
                s = claim(pe, slot["layer2", h, 0])
                for n in range(H2 // P):
                    for c in range(H1 // P):
                        if n == 0:
                            pe.wait_ge(layer_copied, MLP_BANKS * h + c + 1)
                        ins = nc.tensor.matmul(left[:, s, n, :], w2_sb[:, c, n * P:(n + 1) * P], h1[:, c, :],
                                               start=(c == 0), stop=(c == H1 // P - 1))
                    ins.then_inc(layer_summed, 1)

            def layer3(h):
                s = claim(pe, slot["layer3", h, 0])
                for c in range(H2 // P):
                    pe.wait_ge(layer_copied, MLP_BANKS * h + H1 // P + c + 1)
                    ins = nc.tensor.matmul(left[0:1, s, 0, :], w3_sb[:, c:c + 1], h2[:, c, :],
                                           start=(c == 0), stop=(c == H2 // P - 1))
                ins.then_inc(layer_summed, 1)

            for what, n in plan:
                if what == "context":
                    transpose_context(n)
                elif what == "transpose":
                    transpose_x(n)
                elif what == "project":
                    project(n)
                elif what == "reduce":
                    reduce(n)
                elif what in ("layer1_early", "layer1"):
                    layer1(n, what == "layer1_early")
                elif what == "layer2":
                    layer2(n)
                elif what == "layer3":
                    layer3(n)


def kernel(**inputs):
    import concourse.bacc as _bacc
    from concourse.bass_utils import run_bass_kernel_spmd as _run

    nc = _bacc.Bacc("TRN2", target_bir_lowering=False, num_devices=1)
    arrays = {}

    def given(name, a):
        a = np.ascontiguousarray(a)
        arrays[f"in_{name}_dram"] = a
        return nc.dram_tensor(f"in_{name}_dram", a.shape, mybir.dt.from_np(a.dtype), kind="ExternalInput").ap()

    tables = [given(f"tbl_{f}", inputs[f"tbl_{f}"]) for f in range(F)]
    args = [given(n, inputs[n]) for n in ("L0_rec_W", "W_top1", "b_top1", "W_top2", "b_top2", "W_top3")]
    ctx_and_ids = [given(n, inputs[n]) for n in ("dense_ctx", "ids")]
    index = given("w1_rows", w1_rows())
    out = nc.dram_tensor("out_0_dram", (B, 1), F32, kind="ExternalOutput").ap()
    dlrm_tower(nc, *ctx_and_ids, tables, *args, index, out)
    r = _run(nc, [arrays], core_ids=[0])
    return r.results[0]["out_0_dram"]
```
